# Optimizing a Trainium2 kernel written in Bass

```python
import numpy as np
import jax
import jax.numpy as jnp

def _softmax(x, axis=-1):
    return jax.nn.softmax(x, axis=axis)

def _gelu(x):
    return jax.nn.gelu(x, approximate=True)

def _silu(x):
    return jax.nn.silu(x)

def _sigmoid(x):
    return jax.nn.sigmoid(x)

def _layernorm(x, axis=-1, eps=1e-05):
    m = jnp.mean(x, axis=axis, keepdims=True)
    v = jnp.var(x, axis=axis, keepdims=True)
    return (x - m) / jnp.sqrt(v + eps)

def _scatter_add(tgt, idx, src, axis=0):
    return tgt.at[idx].add(src)

def _segment_sum(src, seg, n):
    return jax.ops.segment_sum(src, seg, n)
kernel_name = 'mk_xattn_seq_d1_seqx_r2_d9de99'

def setup_inputs(seed: int=0):
    np.random.seed(seed)
    _w = jnp.asarray

    def _rec_inputs():
        import jax
        import jax.numpy as jnp
        _rk = jax.random.key(seed)
        x = -0.000125 + 0.9999 * jax.random.normal(jax.random.fold_in(_rk, 1), (16, 512, 1024), jnp.float32)
        _lenS = 512 - jax.random.randint(jax.random.fold_in(_rk, 7), (16,), 0, max(1, 512 // 4) + 1, jnp.int32)
        _lenS2 = 512 - jax.random.randint(jax.random.fold_in(_rk, 8), (16,), 0, max(1, 512 // 4) + 1, jnp.int32)
        _ctx_2048P = jax.random.normal(jax.random.fold_in(_rk, 11), (16, 16, 1024), jnp.float32)
        _ctx_2048c = jax.random.dirichlet(jax.random.fold_in(_rk, 511), 0.3 * jnp.ones((16,), jnp.float32), (16, 512))
        _ctx_2048t = jnp.einsum('bsk,bkd->bsd', _ctx_2048c, _ctx_2048P)
        _ctx_2048t = _ctx_2048t * jax.lax.rsqrt(jnp.mean(jnp.square(_ctx_2048t)) + 1e-12) * 0.953939
        ctx_2048 = -1.52775e-05 + 0.999936 * (_ctx_2048t + 0.3 * jax.random.normal(jax.random.fold_in(_rk, 611), (16, 512, 1024), jnp.float32))
        return (x, ctx_2048)
    x, ctx_2048 = _rec_inputs()

    def _L0_xattn_setup():
        import jax, jax.numpy as jnp
        import numpy as np
        B, C, CI, N = (16, 512, 256, 1024)
        EPS = 1e-05

        def _conv1x1(w, b, x):
            return jnp.einsum('oc,bcn->bon', w, x) + b[None, :, None]
        key = jax.random.key(seed)
        ks = jax.random.split(key, 14)
        s = 0.02
        return {'x': jax.random.normal(ks[0], (B, C, N), jnp.float32), 'x_2': jax.random.normal(ks[1], (B, C, N), jnp.float32), 'theta_w': jax.random.normal(ks[2], (CI, C), jnp.float32) * s, 'theta_b': jax.random.normal(ks[3], (CI,), jnp.float32) * s, 'phi_w': jax.random.normal(ks[4], (CI, C), jnp.float32) * s, 'phi_b': jax.random.normal(ks[5], (CI,), jnp.float32) * s, 'g_w': jax.random.normal(ks[6], (CI, C), jnp.float32) * s, 'g_b': jax.random.normal(ks[7], (CI,), jnp.float32) * s, 'w_w': jax.random.normal(ks[8], (C, CI), jnp.float32) * s, 'w_b': jax.random.normal(ks[9], (C,), jnp.float32) * s, 'bn_gamma': jax.random.normal(ks[10], (C,), jnp.float32), 'bn_beta': jax.random.normal(ks[11], (C,), jnp.float32), 'bn_mean': jax.random.normal(ks[12], (C,), jnp.float32), 'bn_var': jax.random.uniform(ks[13], (C,), jnp.float32, 0.5, 1.5)}
    _L0_xattn_all = _L0_xattn_setup()
    _L0_xattn_in = {k: v for k, v in _L0_xattn_all.items() if k in ('theta_w', 'theta_b', 'phi_w', 'phi_b', 'g_w', 'g_b', 'w_w', 'w_b', 'bn_gamma', 'bn_beta', 'bn_mean', 'bn_var')}
    del _L0_xattn_all
    return {'x': x, 'ctx_2048': ctx_2048, 'L0_xattn_theta_w': _L0_xattn_in['theta_w'], 'L0_xattn_theta_b': _L0_xattn_in['theta_b'], 'L0_xattn_phi_w': _L0_xattn_in['phi_w'], 'L0_xattn_phi_b': _L0_xattn_in['phi_b'], 'L0_xattn_g_w': _L0_xattn_in['g_w'], 'L0_xattn_g_b': _L0_xattn_in['g_b'], 'L0_xattn_w_w': _L0_xattn_in['w_w'], 'L0_xattn_w_b': _L0_xattn_in['w_b'], 'L0_xattn_bn_gamma': _L0_xattn_in['bn_gamma'], 'L0_xattn_bn_beta': _L0_xattn_in['bn_beta'], 'L0_xattn_bn_mean': _L0_xattn_in['bn_mean'], 'L0_xattn_bn_var': _L0_xattn_in['bn_var']}

def reference(x, ctx_2048, L0_xattn_theta_w, L0_xattn_theta_b, L0_xattn_phi_w, L0_xattn_phi_b, L0_xattn_g_w, L0_xattn_g_b, L0_xattn_w_w, L0_xattn_w_b, L0_xattn_bn_gamma, L0_xattn_bn_beta, L0_xattn_bn_mean, L0_xattn_bn_var):
    import jax
    import jax.numpy as jnp

    def _L0_xattn_ref(x, x_2, theta_w, theta_b, phi_w, phi_b, g_w, g_b, w_w, w_b, bn_gamma, bn_beta, bn_mean, bn_var):
        import jax, jax.numpy as jnp
        import numpy as np
        B, C, CI, N = (16, 512, 256, 1024)
        EPS = 1e-05

        def _conv1x1(w, b, x):
            return jnp.einsum('oc,bcn->bon', w, x) + b[None, :, None]
        g_x = _conv1x1(g_w, g_b, x_2).transpose(0, 2, 1)
        theta_x = _conv1x1(theta_w, theta_b, x).transpose(0, 2, 1)
        phi_x = _conv1x1(phi_w, phi_b, x_2)
        W = jnp.einsum('bnc,bcm->bnm', theta_x, phi_x) / phi_x.shape[-1]
        y = jnp.einsum('bnm,bmc->bnc', W, g_x).transpose(0, 2, 1)
        wy = _conv1x1(w_w, w_b, y)
        inv_std = jax.lax.rsqrt(bn_var + EPS)
        wy = bn_gamma[None, :, None] * (wy - bn_mean[None, :, None]) * inv_std[None, :, None] + bn_beta[None, :, None]
        return wy + x
    x = _L0_xattn_ref(x, ctx_2048, L0_xattn_theta_w, L0_xattn_theta_b, L0_xattn_phi_w, L0_xattn_phi_b, L0_xattn_g_w, L0_xattn_g_b, L0_xattn_w_w, L0_xattn_w_b, L0_xattn_bn_gamma, L0_xattn_bn_beta, L0_xattn_bn_mean, L0_xattn_bn_var)
    return x

_drawn_inputs = setup_inputs


def setup_inputs(seed=0):
    import zlib

    import numpy as np

    out = dict(_drawn_inputs(seed))
    spreads = {}
    factors = {'L0_xattn_theta_b': 8.0, 'L0_xattn_phi_b': 8.0, 'L0_xattn_g_b': 8.0, 'L0_xattn_w_b': 4.83}
    for name, (base, spread) in spreads.items():
        noise = np.random.default_rng([zlib.crc32(name.encode()), seed]).standard_normal(out[name].shape)
        drawn = base * np.exp(spread * noise) if base else spread * noise
        out[name] = jnp.asarray(drawn.astype(out[name].dtype))
    for name, factor in factors.items():
        out[name] = (out[name] * factor).astype(out[name].dtype)
    return out
```

```python
from contextlib import ExitStack

import concourse.bass as bass
from concourse import mybir

F32 = mybir.dt.float32
F32R = mybir.dt.float32r
BF16 = mybir.dt.bfloat16
ALU = mybir.AluOpType
ACT = mybir.ActivationFunctionType

P = 128
EPS = 1e-5


def xattn_kernel(nc, x, ctx_in, theta_w, theta_b, phi_w, phi_b, g_w, g_b, w_w, w_b,
                 bn_gamma, bn_beta, bn_mean, bn_var, out):
    B, C, N = x.shape
    CI = theta_w.shape[0]
    KC = C // P
    KI = CI // P
    HALF = 512
    NH = N // HALF
    CH = N // P
    QT = 4
    QN = N // QT
    NK = C // 32
    RING = 4
    EARLY = 6
    assert CH * 32 == QN and NH * HALF == N

    ROW0 = [sum((KC - r) * P for r in range(i)) for i in range(KC)]
    UPPER = ROW0[-1] + P
    BANK_OF_ROW = [0, 1, 2, 2]
    BANK_SPAN = [(ROW0[0], ROW0[1]), (ROW0[1], ROW0[2]), (ROW0[2], UPPER)]
    LOWER = [(3, 2), (2, 1), (3, 1), (1, 0), (2, 0), (3, 0)]
    T_BANK = [0, 1, 2, 0]
    Q_BANK = [1, 2]
    T_ORDER = [3, 2, 1, 0]

    NW = 5
    SETUP_GROUPS = 10
    G_S, G_LOW, G_TH, G_OUT = 0, 1, 3, 7
    GROUPS = G_OUT + KC * NH

    def seq(b, pos):
        return b * GROUPS + (SETUP_GROUPS + pos)

    with ExitStack() as ctx:
        def sb(name, shape, dt=F32):
            return ctx.enter_context(nc.sbuf_tensor(name, shape, dt))

        def sem(name):
            return ctx.enter_context(nc.semaphore(name))

        x_sb = [sb(f"x_sb{p}", [P, KC, N]) for p in range(2)]
        ctx_sb = sb("ctx_sb", [P, NK, QN])
        ctxT = sb("ctxT", [P, RING, C])
        ctxT_hi = sb("ctxT_hi", [P, CH, C], F32R)
        ctxT_lo = sb("ctxT_lo", [P, CH, C], F32R)
        x_hi = sb("x_hi", [P, KC, N], F32R)
        x_lo = sb("x_lo", [P, KC, N], F32R)
        th_hi = sb("th_hi", [P, KI, N], F32R)
        th_lo = sb("th_lo", [P, KI, N], F32R)
        gram_hi = sb("gram_hi", [P, UPPER], F32R)
        gram_lo = sb("gram_lo", [P, UPPER], F32R)
        low_hi = sb("low_hi", [P, len(LOWER), P], F32R)
        low_lo = sb("low_lo", [P, len(LOWER), P], F32R)
        stage = sb("stage", [P, UPPER])
        t_hi = sb("t_hi", [P, KC, CI], F32R)
        t_lo = sb("t_lo", [P, KC, CI], F32R)
        q_hi = sb("q_hi", [P, KI, C], F32R)
        q_lo = sb("q_lo", [P, KI, C], F32R)
        wt_hi = sb("wt_hi", [P, KC, CI], F32R)
        wt_lo = sb("wt_lo", [P, KC, CI], F32R)
        wp_hi = sb("wp_hi", [P, KC, CI], F32R)
        wp_lo = sb("wp_lo", [P, KC, CI], F32R)
        z_hi = sb("z_hi", [P, KC, C], F32R)
        z_lo = sb("z_lo", [P, KC, C], F32R)
        phi_nat = sb("phi_nat", [P, KI, C])
        zb_row = sb("zb_row", [P, C])
        bp_row = sb("bp_row", [P, CI])
        ctx_sum = sb("ctx_sum", [P, C])
        sum_hi = sb("sum_hi", [P, C], F32R)
        sum_lo = sb("sum_lo", [P, C], F32R)
        ident = sb("ident", [P, P])
        ones_r = sb("ones_r", [P, P], F32R)
        junk = sb("junk", [P, KI, C], BF16)
        s_col = sb("s_col", [P, KC])
        p1_raw = sb("p1_raw", [P, KI])
        p1 = sb("p1", [P, KI])
        vec_rows = sb("vec_rows", [5 * KC + 3 * KI, P])
        vec_cols = sb("vec_cols", [P, 5 * KC + 3 * KI])
        bt_col, bp_col, bg_col = (vec_cols[:, 5 * KC + i * KI:5 * KC + (i + 1) * KI] for i in range(3))
        nbp_col = sb("nbp_col", [P, KI])
        tmp = sb("tmp", [P, 8, KC])
        const = sb("const", [P, KC])
        scale = sb("scale", [P, KC])
        g_nat = x_sb[1][:, 0, :].rearrange("p (k c) -> p k c", k=KI)
        w_nat = x_sb[1][:, 1, :].rearrange("p (m c) -> p m c", m=KC)
        ws_nat = x_sb[1][:, 2, :].rearrange("p (m c) -> p m c", m=KC)
        wsT = x_sb[1][:, 3, :].rearrange("p (k o) -> p k o", k=KI)
        theta_nat = stage[:, 0:KI * C].rearrange("p (k c) -> p k c", k=KI)
        bg_wide = stage[:, KI * C:KI * C + KI * P].rearrange("p (k c) -> p k c", k=KI)

        gbank = [ctx.enter_context(nc.psum_tensor(f"gbank{i}", [P, HALF], F32)) for i in range(3)]
        wbank = [ctx.enter_context(nc.psum_tensor(f"wbank{i}", [P, HALF], F32)) for i in range(NW)]

        def bank(pos):
            return wbank[(SETUP_GROUPS + pos) % NW]

        in_w1, in_w2, in_w3, in_vec, in_bp = (sem(n) for n in ("in_w1", "in_w2", "in_w3", "in_vec", "in_bp"))
        in_w4 = sem("in_w4")
        in_ctx = sem("in_ctx")
        in_x = [sem(f"in_x{p}") for p in range(2)]
        stored = sem("stored")
        ident_done, ones_done = sem("ident_done"), sem("ones_done")
        vec_step = sem("vec_step")
        vec_turned = sem("vec_turned")
        root_done = sem("root_done")
        wide_done = sem("wide_done")
        zb_done, zb_taken = sem("zb_done"), sem("zb_taken")
        split_hi = sem("split_hi")
        ctxT_made = sem("ctxT_made")
        ctxT_hi_made = sem("ctxT_hi_made")
        ctxT_lo_made = sem("ctxT_lo_made")
        ctxT_used = sem("ctxT_used")
        sum_split = sem("sum_split")
        x_hi_made, x_lo_made = sem("x_hi_made"), sem("x_lo_made")
        gram_chunk = sem("gram_chunk")
        gram_row = sem("gram_row")
        gram_f32 = sem("gram_f32")
        gram_hi_made, gram_lo_made = sem("gram_hi_made"), sem("gram_lo_made")
        low_hi_made = sem("low_hi_made")
        s_made = sem("s_made")
        th_hi_made = sem("th_hi_made")
        t_done, t_taken, t_hi_made, t_lo_made = (sem(n) for n in ("t_done", "t_taken", "t_hi_made", "t_lo_made"))
        q_done, q_taken, q_hi_made, q_lo_made = (sem(n) for n in ("q_done", "q_taken", "q_hi_made", "q_lo_made"))
        work_done = sem("work_done")
        work_free = sem("work_free")

        def f(ap):
            return ap.bitcast(F32)

        def upper(tile, j, i):
            at = ROW0[j] + (i - j) * P
            return tile[:, at:at + P]

        def gram_block(up, low, j, i):
            return upper(up, j, i) if j <= i else low[:, LOWER.index((j, i)), :]

        def batches(eng, body):
            with_pairs = (B - 2) // 2
            with eng.Fori(0, with_pairs) as t:
                body(2 * t, t, 0, True, True)
                body(2 * t + 1, t, 1, True, True)
            body(B - 2, B // 2 - 1, 0, True, False)
            body(B - 1, B // 2 - 1, 1, False, False)

        block = ctx.enter_context(nc.Block())

        @block.sync
        def _(sp):
            def load_ctx(b):
                src = ctx_in[b].rearrange("(k q) (a n) -> a q k n", q=32, a=QT)
                for a in range(QT):
                    sp.dma_start(ctx_sb[32 * a:32 * a + 32, :, :], src[a]).then_inc(in_ctx, 16)

            def load_x(b, par):
                sp.dma_start(x_sb[par][:, :, :], x[b].rearrange("(m p) n -> p m n", p=P)).then_inc(in_x[par], 16)

            sp.dma_start(w_nat, w_w.rearrange("(m p) c -> p m c", p=P)).then_inc(in_w1, 16)
            row = 0
            for v in (w_b, bn_gamma, bn_beta, bn_mean, bn_var, theta_b, phi_b, g_b):
                rows = v.shape[0] // P
                sp.dma_start(vec_rows[row:row + rows, :], v.rearrange("(m p) -> m p", p=P)).then_inc(in_vec, 16)
                row += rows
            sp.dma_start(g_nat, g_w.rearrange("(k p) c -> p k c", p=P)).then_inc(in_w2, 16)
            load_ctx(0)
            sp.dma_start(phi_nat[:, :, :], phi_w.rearrange("(k p) c -> p k c", p=P)).then_inc(in_w3, 16)
            sp.dma_start(theta_nat, theta_w.rearrange("(k p) c -> p k c", p=P)).then_inc(in_w4, 16)
            sp.dma_start(bp_row[:, :], phi_b.partition_broadcast(P)).then_inc(in_bp, 16)
            load_x(0, 0)
            sp.wait_ge(ctxT_made, CH)
            load_ctx(1)
            sp.wait_ge(work_done, SETUP_GROUPS - 4)
            sp.wait_ge(zb_done, 1)
            load_x(1, 1)

            def body(b, half, par, nxt, nxt2):
                if nxt2:
                    sp.wait_ge(ctxT_made, CH * b + 2 * CH)
                    load_ctx(b + 2)
                for m in range(KC):
                    sp.wait_ge(work_free, seq(b, G_OUT + NH * (m + 1)))
                    sp.dma_start(out[b].rearrange("(m p) n -> m p n", p=P)[m], x_sb[par][:, m, :]).then_inc(stored, 16)
                if nxt2:
                    sp.wait_ge(stored, b * (16 * KC) + 16 * KC)
                    load_x(b + 2, par)

            batches(sp, body)
            sp.wait_ge(stored, 16 * KC * B)

        @block.gpsimd
        def _(pool):
            nc.gpsimd.memset(ident[:, :], 0.0).then_inc(ident_done, 1)
            pool.wait_ge(ident_done, 1)
            nc.gpsimd.affine_select(out=ident[:, :], in_=ident[:, :], compare_op=ALU.not_equal, fill=1.0, base=0,
                                    pattern=[[-1, P]], channel_multiplier=1).then_inc(ident_done, 1)
            nc.gpsimd.memset(ones_r[:, :].bitcast(F32), 1.0).then_inc(ones_done, 1)

            def prep_ctx(b, first=False):
                for c in range(CH):
                    src = ctxT[:, c % RING, :]
                    if first:
                        pool.wait_ge(ctxT_made, c + 1)
                    else:
                        if c == 0:
                            pool.wait_ge(sum_split, 2 * b)
                        pool.wait_ge(ctxT_hi_made, CH * b + (c + 1))
                        nc.gpsimd.tensor_tensor(ctxT_lo[:, c, :], src, f(ctxT_hi[:, c, :]),
                                                ALU.subtract).then_inc(ctxT_lo_made, 1)
                    if c == 0:
                        nc.gpsimd.tensor_copy(ctx_sum[:, :], src).then_inc(ctxT_used, 1)
                    else:
                        pool.wait_ge(ctxT_used, CH * b + c)
                        if c == CH - 1:
                            nc.gpsimd.tensor_tensor(sum_hi[:, :], ctx_sum[:, :], src, ALU.add).then_inc(sum_split, 1)
                        nc.gpsimd.tensor_tensor(ctx_sum[:, :], ctx_sum[:, :], src, ALU.add).then_inc(ctxT_used, 1)
                pool.wait_ge(ctxT_used, CH * b + CH)
                pool.wait_ge(sum_split, 2 * b + 1)
                nc.gpsimd.tensor_tensor(sum_lo[:, :], ctx_sum[:, :], f(sum_hi[:, :]), ALU.subtract).then_inc(sum_split, 1)

            def prep_x(b, par):
                for k in range(KC):
                    pool.wait_ge(x_hi_made, KC * b + (k + 1))
                    nc.gpsimd.tensor_tensor(x_lo[:, k, :], x_sb[par][:, k, :], f(x_hi[:, k, :]),
                                            ALU.subtract).then_inc(x_lo_made, 1)

            prep_ctx(0, first=True)
            prep_x(0, 0)

            def body(b, half, par, nxt, nxt2):
                if nxt:
                    prep_ctx(b + 1)
                    prep_x(b + 1, 1 - par)

            batches(pool, body)

        @block.scalar
        def _(act):
            def hi(dst, src, sem_):
                nc.scalar.activation(dst, src, ACT.Copy).then_inc(sem_, 1)

            def ctx_hi(b, c):
                act.wait_ge(ctxT_made, CH * b + (c + 1))
                hi(ctxT_hi[:, c, :], ctxT[:, c % RING, :], ctxT_hi_made)

            def prep_x(b, half, par):
                act.wait_ge(in_x[par], 16 * half + 16)
                for k in range(KC):
                    hi(x_hi[:, k, :], x_sb[par][:, k, :], x_hi_made)

            act.wait_ge(vec_step, 2)
            nc.scalar.activation(tmp[:, 1, :], tmp[:, 0, :], ACT.Sqrt).then_inc(root_done, 1)
            for c in range(CH):
                ctx_hi(0, c)
            for g in range(KC):
                act.wait_ge(work_done, 3 + g)
                hi(z_hi[:, g, :], wbank[(2 + g) % NW][:, :], split_hi)
            for g, dst in ((6, wp_hi[:, 0:2, :]), (7, wp_hi[:, 2:4, :]), (8, wt_hi[:, 0:2, :]), (9, wt_hi[:, 2:4, :])):
                act.wait_ge(work_done, g + 1)
                hi(dst, wbank[g % NW][:, :].rearrange("p (k c) -> p k c", k=2), split_hi)
            prep_x(0, 0, 0)

            def body(b, half, par, nxt, nxt2):
                if nxt:
                    for c in range(EARLY):
                        act.wait_ge(gram_chunk, (CH - 1) * b + (c + 1))
                        ctx_hi(b + 1, c)
                for i, (a, z) in enumerate(BANK_SPAN):
                    act.wait_ge(gram_row, 3 * b + (i + 1))
                    hi(stage[:, a:z], gbank[i][:, 0:z - a], gram_f32)
                for g in range(2):
                    act.wait_ge(work_done, seq(b, G_LOW + g + 1))
                    hi(low_hi[:, 3 * g:3 * g + 3, :],
                       bank(G_LOW + g)[:, 0:3 * P].rearrange("p (j c) -> p j c", j=3), low_hi_made)

                def theta(m):
                    for h in range(NH):
                        act.wait_ge(work_done, seq(b, G_TH + NH * m + h + 1))
                        nc.scalar.activation(th_hi[:, m, h * HALF:(h + 1) * HALF], bank(G_TH + NH * m + h)[:, :],
                                             ACT.Identity, bias=bt_col[:, m:m + 1]).then_inc(th_hi_made, 1)

                theta(0)
                if nxt:
                    for c in range(EARLY, CH):
                        ctx_hi(b + 1, c)
                for r, m in enumerate(T_ORDER):
                    act.wait_ge(t_taken, KC * b + (r + 1))
                    hi(t_hi[:, m, :], stage[:, r * CI:(r + 1) * CI], t_hi_made)
                for k in range(KI):
                    act.wait_ge(q_taken, KI * b + (k + 1))
                    hi(q_hi[:, k, :], stage[:, k * C:(k + 1) * C], q_hi_made)
                theta(1)
                if nxt:
                    prep_x(b + 1, half + (1 if par else 0), 1 - par)

            batches(act, body)

        @block.vector
        def _(dve):
            steps = [0]

            def chain(ins):
                steps[0] += 1
                ins.then_inc(vec_step, 1)
                dve.wait_ge(vec_step, steps[0])

            def transpose_chunk(b, c, free):
                if free:
                    dve.wait_ge(ctxT_used, CH * b + (c + 1 - RING))
                nc.vector.transpose(ctxT[:, c % RING, :].rearrange("p (k q) -> p k q", q=32),
                                    ctx_sb[:, :, 32 * c:32 * c + 32]).then_inc(ctxT_made, 1)

            dve.wait_ge(vec_turned, 1)
            chain(nc.vector.tensor_copy(vec_cols[:, :], gbank[1][:, 0:5 * KC + 3 * KI]))
            wb_, gamma_, beta_, mean_, var_ = (vec_cols[:, i * KC:(i + 1) * KC] for i in range(5))
            ve, root, r0, r2, r3, r4, wm = (tmp[:, i, :] for i in range(7))
            chain(nc.vector.tensor_scalar(ve, var_, EPS, None, ALU.add))
            dve.wait_ge(root_done, 1)
            chain(nc.vector.reciprocal(r0, root))
            chain(nc.vector.tensor_tensor(r2, r0, r0, ALU.mult))
            chain(nc.vector.tensor_tensor(r3, r2, ve, ALU.mult))
            chain(nc.vector.tensor_scalar(r4, r3, -0.5, 1.5, ALU.mult, ALU.add))
            chain(nc.vector.tensor_tensor(r2, r0, r4, ALU.mult))
            chain(nc.vector.tensor_tensor(scale[:, :], r2, gamma_, ALU.mult))
            chain(nc.vector.tensor_tensor(wm, wb_, mean_, ALU.subtract))
            chain(nc.vector.tensor_tensor(r3, wm, scale[:, :], ALU.mult))
            chain(nc.vector.tensor_tensor(const[:, :], r3, beta_, ALU.add))
            nc.vector.tensor_scalar(nbp_col[:, :], bp_col[:, :], float(N), None, ALU.mult).then_inc(wide_done, 1)
            dve.wait_ge(in_w1, 16)
            for m in range(KC):
                nc.vector.tensor_scalar(ws_nat[:, m, :], w_nat[:, m, :], scale[:, m:m + 1], 1.0 / N,
                                        ALU.mult, ALU.mult).then_inc(wide_done, 1)
            dve.wait_ge(ones_done, 1)
            for k in range(KI):
                nc.vector.tensor_scalar(bg_wide[:, k, :], f(ones_r[:, :]), bg_col[:, k:k + 1], None,
                                        ALU.mult).then_inc(wide_done, 1)
            for k in range(KI):
                dve.wait_ge(work_done, k + 1)
                nc.vector.tensor_copy(wsT[:, k, :], wbank[k][:, :]).then_inc(work_free, 1)
            dve.wait_ge(in_ctx, 16 * QT)

            def first_lo(c):
                dve.wait_ge(ctxT_hi_made, c + 1)
                nc.vector.tensor_tensor(ctxT_lo[:, c, :], ctxT[:, c % RING, :], f(ctxT_hi[:, c, :]),
                                        ALU.subtract).then_inc(ctxT_lo_made, 1)

            for c in range(CH):
                transpose_chunk(0, c, c >= RING)
                if c > 0:
                    first_lo(c - 1)
            first_lo(CH - 1)
            for g in range(KC):
                dve.wait_ge(split_hi, g + 1)
                nc.vector.tensor_tensor(z_lo[:, g, :], wbank[(2 + g) % NW][:, :], f(z_hi[:, g, :]),
                                        ALU.subtract).then_inc(work_free, 1)
            dve.wait_ge(zb_done, 1)
            nc.vector.tensor_copy(zb_row[:, :], gbank[0][:, :]).then_inc(zb_taken, 1)
            for g, dh, dl in ((6, wp_hi[:, 0:2, :], wp_lo[:, 0:2, :]), (7, wp_hi[:, 2:4, :], wp_lo[:, 2:4, :]),
                              (8, wt_hi[:, 0:2, :], wt_lo[:, 0:2, :]), (9, wt_hi[:, 2:4, :], wt_lo[:, 2:4, :])):
                dve.wait_ge(split_hi, g - 1)
                nc.vector.tensor_tensor(dl, wbank[g % NW][:, :].rearrange("p (k c) -> p k c", k=2), f(dh),
                                        ALU.subtract).then_inc(work_free, 1)
            dve.wait_ge(in_bp, 16)

            def body(b, half, par, nxt, nxt2):
                if nxt:
                    dve.wait_ge(in_ctx, b * (16 * QT) + 32 * QT)
                    for c in range(EARLY):
                        transpose_chunk(b + 1, c, True)
                dve.wait_ge(work_done, seq(b, G_S + 1))
                s_all = bank(G_S)
                for i in range(KC):
                    nc.vector.tensor_tensor_reduce(junk[:, 0, i * P:(i + 1) * P], s_all[:, i * P:(i + 1) * P], ident[:, :], 1.0, 0.0,
                                                   ALU.mult, ALU.add, s_col[:, i:i + 1]).then_inc(s_made, 1)
                for k in range(KI):
                    if k == 1:
                        dve.wait_ge(s_made, 6 * b + KC)
                    ins = nc.vector.tensor_tensor_reduce(junk[:, 1 - k, :], s_all[:, :], phi_nat[:, k, :], 1.0, 0.0,
                                                         ALU.mult, ALU.add, p1_raw[:, k:k + 1])
                    ins.then_inc(s_made, 1)
                dve.wait_ge(s_made, 6 * b + 6)
                nc.vector.tensor_tensor(p1[:, :], p1_raw[:, :], nbp_col[:, :], ALU.add).then_inc(work_free, 1)
                for i, (a, z) in enumerate(BANK_SPAN):
                    dve.wait_ge(gram_f32, 3 * b + (i + 1))
                    nc.vector.tensor_copy(gram_hi[:, a:z], stage[:, a:z]).then_inc(gram_hi_made, 1)
                    dve.wait_ge(gram_hi_made, 3 * b + (i + 1))
                    nc.vector.tensor_tensor(gram_lo[:, a:z], stage[:, a:z], f(gram_hi[:, a:z]),
                                            ALU.subtract).then_inc(gram_lo_made, 1)
                for g in range(2):
                    dve.wait_ge(low_hi_made, 2 * b + (g + 1))
                    nc.vector.tensor_tensor(low_lo[:, 3 * g:3 * g + 3, :],
                                            bank(G_LOW + g)[:, 0:3 * P].rearrange("p (j c) -> p j c", j=3),
                                            f(low_hi[:, 3 * g:3 * g + 3, :]),
                                            ALU.subtract).then_inc(work_free, 1)

                def theta(m):
                    for h in range(NH):
                        dve.wait_ge(th_hi_made, KI * NH * b + (NH * m + h + 1))
                        cols = slice(h * HALF, (h + 1) * HALF)
                        nc.vector.scalar_tensor_tensor(out=th_lo[:, m, cols], in0=bank(G_TH + NH * m + h)[:, :],
                                                       scalar=bt_col[:, m:m + 1], in1=f(th_hi[:, m, cols]),
                                                       op0=ALU.add, op1=ALU.subtract).then_inc(work_free, 1)

                theta(0)
                if nxt:
                    for c in range(EARLY, CH):
                        transpose_chunk(b + 1, c, True)

                def t_lo_part(r):
                    m = T_ORDER[r]
                    dve.wait_ge(t_hi_made, KC * b + (r + 1))
                    nc.vector.tensor_tensor(t_lo[:, m, :], stage[:, r * CI:(r + 1) * CI], f(t_hi[:, m, :]),
                                            ALU.subtract).then_inc(t_lo_made, 1)

                for r, m in enumerate(T_ORDER):
                    dve.wait_ge(t_done, KC * b + (r + 1))
                    nc.vector.scalar_tensor_tensor(out=stage[:, r * CI:(r + 1) * CI], in0=bp_row[:, :],
                                                   scalar=s_col[:, m:m + 1],
                                                   in1=gbank[T_BANK[r]][:, 0:CI],
                                                   op0=ALU.mult, op1=ALU.add).then_inc(t_taken, 1)
                    if r > 0:
                        t_lo_part(r - 1)
                t_lo_part(KC - 1)

                def q_lo_part(k):
                    dve.wait_ge(q_hi_made, KI * b + (k + 1))
                    nc.vector.tensor_tensor(q_lo[:, k, :], stage[:, k * C:(k + 1) * C], f(q_hi[:, k, :]),
                                            ALU.subtract).then_inc(q_lo_made, 1)

                dve.wait_ge(work_free, seq(b, G_S + 1))
                for k in range(KI):
                    dve.wait_ge(q_done, KI * b + (k + 1))
                    nc.vector.scalar_tensor_tensor(out=stage[:, k * C:(k + 1) * C], in0=zb_row[:, :],
                                                   scalar=p1[:, k:k + 1], in1=gbank[Q_BANK[k]][:, :],
                                                   op0=ALU.mult, op1=ALU.add).then_inc(q_taken, 1)
                    if k > 0:
                        q_lo_part(k - 1)
                q_lo_part(KI - 1)
                theta(1)
                for m in range(KC):
                    for h in range(NH):
                        pos = G_OUT + NH * m + h
                        cols = slice(h * HALF, (h + 1) * HALF)
                        dve.wait_ge(work_done, seq(b, pos + 1))
                        nc.vector.scalar_tensor_tensor(out=x_sb[par][:, m, cols], in0=bank(pos)[:, :],
                                                       scalar=const[:, m:m + 1], in1=x_sb[par][:, m, cols],
                                                       op0=ALU.add, op1=ALU.add).then_inc(work_free, 1)

            batches(dve, body)

        @block.tensor
        def _(pe):
            def mm(dst, lhsT, rhs, start, stop):
                return nc.tensor.matmul(dst, lhsT, rhs, start=start, stop=stop, skip_group_check=True)

            def setup():
                pe.wait_ge(ident_done, 2)
                pe.wait_ge(in_vec, 16 * 8)
                rows = 5 * KC + 3 * KI
                nc.tensor.transpose(gbank[1][:, 0:rows], vec_rows[:, :], ident[0:rows, 0:rows]).then_inc(vec_turned, 1)
                pe.wait_ge(wide_done, 1 + KC)
                for k in range(KI):
                    for m in range(KC):
                        ins = nc.tensor.transpose(wbank[k][:, m * P:(m + 1) * P], ws_nat[:, m, k * P:(k + 1) * P],
                                                  ident[:, :])
                    ins.then_inc(work_done, 1)
                pe.wait_ge(in_w2, 16)
                pe.wait_ge(work_free, KI)
                for j in range(KC):
                    for k in range(KI):
                        ins = nc.tensor.matmul(wbank[(2 + j) % NW][:, :], g_nat[:, k, j * P:(j + 1) * P], wsT[:, k, :],
                                               start=k == 0, stop=k == KI - 1)
                    ins.then_inc(work_done, 1)
                pe.wait_ge(wide_done, 1 + KC + KI)
                for k in range(KI):
                    ins = nc.tensor.matmul(gbank[0][:, :], bg_wide[:, k, :], wsT[:, k, :], start=k == 0,
                                           stop=k == KI - 1)
                ins.then_inc(zb_done, 1)
                for name, nat, first in ((in_w3, phi_nat, 6), (in_w4, theta_nat, 8)):
                    pe.wait_ge(name, 16)
                    for g in range(2):
                        pe.wait_ge(work_free, first + g - NW + 1)
                        for j in range(2):
                            for k in range(KI):
                                c = 2 * g + j
                                ins = nc.tensor.transpose(
                                    wbank[(first + g) % NW][:, j * CI + k * P:j * CI + (k + 1) * P],
                                    nat[:, k, c * P:(c + 1) * P], ident[:, :])
                        ins.then_inc(work_done, 1)

            setup()
            pe.wait_ge(zb_taken, 1)

            def body(b, half, par, nxt, nxt2):
                def own(pos):
                    pe.wait_ge(work_free, seq(b, pos - NW + 1))

                for c in range(CH):
                    pe.wait_ge(ctxT_lo_made, CH * b + (c + 1))
                    for i in range(KC):
                        base = 0 if i < 3 else ROW0[3] - ROW0[2]
                        dst = gbank[BANK_OF_ROW[i]][:, base:base + C - i * P]
                        h_i = ctxT_hi[:, c, i * P:(i + 1) * P]
                        l_i = ctxT_lo[:, c, i * P:(i + 1) * P]
                        mm(dst, h_i, ctxT_hi[:, c, i * P:], c == 0 and i < 3, False)
                        mm(dst, h_i, ctxT_lo[:, c, i * P:], False, False)
                        ins = mm(dst, l_i, ctxT_hi[:, c, i * P:], False, c == CH - 1)
                        if c == CH - 1 and i != 2:
                            ins.then_inc(gram_row, 1)
                    if c < CH - 1:
                        ins.then_inc(gram_chunk, 1)
                    if c == CH - 3:
                        own(G_S)
                        pe.wait_ge(sum_split, 2 * b + 2)
                        mm(bank(G_S)[:, :], ones_r[:, :], sum_hi[:, :], True, False)
                        mm(bank(G_S)[:, :], ones_r[:, :], sum_lo[:, :], False, True).then_inc(work_done, 1)

                def theta(m, ks):
                    for k in ks:
                        if k == 0:
                            for h in range(NH):
                                own(G_TH + NH * m + h)
                        if m == 0:
                            pe.wait_ge(x_lo_made, KC * b + (k + 1))
                        w_h, w_l = wt_hi[:, k, m * P:(m + 1) * P], wt_lo[:, k, m * P:(m + 1) * P]
                        for w, src in ((w_h, x_hi), (w_h, x_lo), (w_l, x_hi)):
                            for h in range(NH):
                                last = k == KC - 1 and w is w_l
                                ins = mm(bank(G_TH + NH * m + h)[:, :], w, src[:, k, h * HALF:(h + 1) * HALF],
                                         k == 0 and src is x_hi and w is w_h, last)
                                if last:
                                    ins.then_inc(work_done, 1)

                def t_block(r):
                    m = T_ORDER[r]
                    dst = gbank[T_BANK[r]][:, 0:CI]
                    for j in range(KC):
                        g_h, g_l = gram_block(gram_hi, low_hi, j, m), gram_block(gram_lo, low_lo, j, m)
                        mm(dst, g_h, wp_hi[:, j, :], j == 0, False)
                        mm(dst, g_h, wp_lo[:, j, :], False, False)
                        ins = mm(dst, g_l, wp_hi[:, j, :], False, j == KC - 1)
                    ins.then_inc(t_done, 1)

                theta(0, (0, 1))
                pe.wait_ge(gram_f32, 3 * b + 3)
                for g in range(2):
                    own(G_LOW + g)
                    for n in range(3):
                        j, i = LOWER[3 * g + n]
                        ins = nc.tensor.transpose(bank(G_LOW + g)[:, n * P:(n + 1) * P], upper(stage, i, j), ident[:, :])
                    ins.then_inc(work_done, 1)
                theta(0, (2, 3))
                pe.wait_ge(gram_lo_made, 3 * b + 3)
                t_block(0)
                pe.wait_ge(work_free, seq(b, G_LOW + 1))
                t_block(1)
                t_block(2)
                pe.wait_ge(work_free, seq(b, G_LOW + 2))
                pe.wait_ge(t_taken, KC * b + 1)
                t_block(3)
                theta(1, (0, 1))
                pe.wait_ge(t_taken, KC * b + 3)
                for r, j in enumerate(T_ORDER):
                    pe.wait_ge(t_lo_made, KC * b + (r + 1))
                    for k in range(KI):
                        dst = gbank[Q_BANK[k]][:, :]
                        t_h, t_l = t_hi[:, j, k * P:(k + 1) * P], t_lo[:, j, k * P:(k + 1) * P]
                        mm(dst, t_h, z_hi[:, j, :], r == 0, False)
                        mm(dst, t_h, z_lo[:, j, :], False, False)
                        ins = mm(dst, t_l, z_hi[:, j, :], False, r == KC - 1)
                        if r == KC - 1:
                            ins.then_inc(q_done, 1)
                theta(1, (2, 3))

                def out_part(m, k):
                    if k == 0:
                        for h in range(NH):
                            own(G_OUT + NH * m + h)
                    q_h, q_l = q_hi[:, k, m * P:(m + 1) * P], q_lo[:, k, m * P:(m + 1) * P]
                    for w, src in ((q_h, th_hi), (q_h, th_lo), (q_l, th_hi)):
                        for h in range(NH):
                            last = k == KI - 1 and w is q_l
                            ins = mm(bank(G_OUT + NH * m + h)[:, :], w, src[:, k, h * HALF:(h + 1) * HALF],
                                     k == 0 and src is th_hi and w is q_h, last)
                            if last:
                                ins.then_inc(work_done, 1)

                pe.wait_ge(q_lo_made, KI * b + 1)
                out_part(0, 0)
                out_part(1, 0)
                pe.wait_ge(q_lo_made, KI * b + 2)
                pe.wait_ge(work_free, seq(b, G_TH + KI * NH))
                out_part(0, 1)
                out_part(1, 1)
                for m in (2, 3):
                    out_part(m, 0)
                    out_part(m, 1)

            batches(pe, body)


_INS = ['x', 'ctx_2048', 'L0_xattn_theta_w', 'L0_xattn_theta_b', 'L0_xattn_phi_w', 'L0_xattn_phi_b',
        'L0_xattn_g_w', 'L0_xattn_g_b', 'L0_xattn_w_w', 'L0_xattn_w_b', 'L0_xattn_bn_gamma',
        'L0_xattn_bn_beta', 'L0_xattn_bn_mean', 'L0_xattn_bn_var']
_OUT = ((16, 512, 1024), 'float32')


def kernel(**inputs):
    import numpy as _np
    import concourse.bacc as _bacc
    from concourse import mybir as _mybir
    from concourse.bass_utils import run_bass_kernel_spmd as _run

    nc = _bacc.Bacc("TRN2", target_bir_lowering=False, num_devices=1, dynamic_dma_scratch_size=1024)
    arrays, args = {}, []
    for name in _INS:
        a = _np.ascontiguousarray(inputs[name])
        arrays[f"in_{name}_dram"] = a
        args.append(nc.dram_tensor(f"in_{name}_dram", a.shape, _mybir.dt.from_np(a.dtype), kind="ExternalInput").ap())
    shape, dtype = _OUT
    args.append(nc.dram_tensor("out_0_dram", shape, _mybir.dt.from_np(_np.dtype(dtype)), kind="ExternalOutput").ap())
    xattn_kernel(nc, *args)
    r = _run(nc, [arrays], core_ids=[0])
    return r.results[0]["out_0_dram"]
```
